# Optimizing a Trainium2 kernel written in Bass

```python
import numpy as np
import jax
import jax.numpy as jnp

def _softmax(x, axis=-1):
    return jax.nn.softmax(x, axis=axis)

def _gelu(x):
    return jax.nn.gelu(x, approximate=True)

def _silu(x):
    return jax.nn.silu(x)

def _sigmoid(x):
    return jax.nn.sigmoid(x)

def _layernorm(x, axis=-1, eps=1e-05):
    m = jnp.mean(x, axis=axis, keepdims=True)
    v = jnp.var(x, axis=axis, keepdims=True)
    return (x - m) / jnp.sqrt(v + eps)

def _scatter_add(tgt, idx, src, axis=0):
    return tgt.at[idx].add(src)

def _segment_sum(src, seg, n):
    return jax.ops.segment_sum(src, seg, n)
kernel_name = 'mk_seq_postln_d1_jaxref_r8_d09752'

def setup_inputs(seed: int=0):
    np.random.seed(seed)
    _w = jnp.asarray

    def _L0_attn_setup():
        import jax, jax.numpy as jnp
        import numpy as np
        D_MODEL = 128
        N_HEADS = 16
        N_KV = 4
        HEAD_DIM = D_MODEL // N_HEADS
        SEQ = 256
        BATCH = 2
        CAP = 50.0
        EPS = 1e-05
        THETA = 10000.0

        def _rms_norm(x, eps=EPS):
            return x * jax.lax.rsqrt(jnp.mean(jnp.square(x), axis=-1, keepdims=True) + eps)

        def _rope_cos_sin(seq_len, head_dim, theta=THETA):
            inv_freq = 1.0 / theta ** (jnp.arange(0, head_dim, 2, dtype=jnp.float32) / head_dim)
            freqs = jnp.arange(seq_len, dtype=jnp.float32)[:, None] * inv_freq[None, :]
            return (jnp.cos(freqs)[None, :, None, :], jnp.sin(freqs)[None, :, None, :])

        def _apply_rope(x, cos, sin):
            d = x.shape[-1] // 2
            x1, x2 = (x[..., :d], x[..., d:])
            return jnp.concatenate([x1 * cos - x2 * sin, x2 * cos + x1 * sin], axis=-1).astype(x.dtype)
        key = jax.random.key(seed)
        ks = jax.random.split(key, 5)
        s = 0.02
        return {'x': jax.random.normal(ks[0], (BATCH, SEQ, D_MODEL), dtype=jnp.float32), 'w_q': jax.random.normal(ks[1], (D_MODEL, N_HEADS * HEAD_DIM), dtype=jnp.float32) * s, 'w_k': jax.random.normal(ks[2], (D_MODEL, N_KV * HEAD_DIM), dtype=jnp.float32) * s, 'w_v': jax.random.normal(ks[3], (D_MODEL, N_KV * HEAD_DIM), dtype=jnp.float32) * s, 'w_o': jax.random.normal(ks[4], (N_HEADS * HEAD_DIM, D_MODEL), dtype=jnp.float32) * s}
    _L0_attn_in = _L0_attn_setup()

    def _L0_ffn_setup():
        import jax, jax.numpy as jnp
        import numpy as np
        B, S, H, NH, E, F = (4, 128, 128, 16, 8, 512)
        D = H // NH
        EPS = 1e-05

        def _layernorm(x, g, b):
            mu = jnp.mean(x, axis=-1, keepdims=True)
            var = jnp.var(x, axis=-1, keepdims=True)
            return (x - mu) * jax.lax.rsqrt(var + EPS) * g + b
        key = jax.random.key(seed)
        ks = jax.random.split(key, 16)
        s = 0.02
        return {'x': jax.random.normal(ks[0], (B, S, H), jnp.float32), 'ln1_g': jnp.ones((H,), jnp.float32), 'ln1_b': jnp.zeros((H,), jnp.float32), 'ln2_g': jnp.ones((H,), jnp.float32), 'ln2_b': jnp.zeros((H,), jnp.float32), 'wq': jax.random.normal(ks[1], (H, H), jnp.float32) * s, 'bq': jnp.zeros((H,), jnp.float32), 'wk': jax.random.normal(ks[2], (H, H), jnp.float32) * s, 'bk': jnp.zeros((H,), jnp.float32), 'wv': jax.random.normal(ks[3], (H, H), jnp.float32) * s, 'bv': jnp.zeros((H,), jnp.float32), 'wo': jax.random.normal(ks[4], (H, H), jnp.float32) * s, 'bo': jnp.zeros((H,), jnp.float32), 'gate_w': jax.random.normal(ks[5], (H, E), jnp.float32) * s, 'gate_b': jnp.zeros((E,), jnp.float32), 'w1': jax.random.normal(ks[6], (E, H, F), jnp.float32) * s, 'b1': jnp.zeros((E, F), jnp.float32), 'w2': jax.random.normal(ks[7], (E, F, H), jnp.float32) * s, 'b2': jnp.zeros((E, H), jnp.float32)}
    _L0_ffn_in = _L0_ffn_setup()
    _d = {'L0_attn_x': _L0_attn_in['x'], 'L0_attn_w_q': _L0_attn_in['w_q'], 'L0_attn_w_k': _L0_attn_in['w_k'], 'L0_attn_w_v': _L0_attn_in['w_v'], 'L0_attn_w_o': _L0_attn_in['w_o'], 'L0_ffn_ln1_g': _L0_ffn_in['ln1_g'], 'L0_ffn_ln1_b': _L0_ffn_in['ln1_b'], 'L0_ffn_ln2_g': _L0_ffn_in['ln2_g'], 'L0_ffn_ln2_b': _L0_ffn_in['ln2_b'], 'L0_ffn_wq': _L0_ffn_in['wq'], 'L0_ffn_bq': _L0_ffn_in['bq'], 'L0_ffn_wk': _L0_ffn_in['wk'], 'L0_ffn_bk': _L0_ffn_in['bk'], 'L0_ffn_wv': _L0_ffn_in['wv'], 'L0_ffn_bv': _L0_ffn_in['bv'], 'L0_ffn_wo': _L0_ffn_in['wo'], 'L0_ffn_bo': _L0_ffn_in['bo'], 'L0_ffn_gate_w': _L0_ffn_in['gate_w'], 'L0_ffn_gate_b': _L0_ffn_in['gate_b'], 'L0_ffn_w1': _L0_ffn_in['w1'], 'L0_ffn_b1': _L0_ffn_in['b1'], 'L0_ffn_w2': _L0_ffn_in['w2'], 'L0_ffn_b2': _L0_ffn_in['b2']}
    _x0 = _d['L0_attn_x']
    _d['L0_attn_x'] = jax.random.normal(jax.random.fold_in(jax.random.key(seed), 1), (16, 256, 128), dtype=_x0.dtype)
    del _x0
    return _d

def reference(L0_attn_x, L0_attn_w_q, L0_attn_w_k, L0_attn_w_v, L0_attn_w_o, L0_ffn_ln1_g, L0_ffn_ln1_b, L0_ffn_ln2_g, L0_ffn_ln2_b, L0_ffn_wq, L0_ffn_bq, L0_ffn_wk, L0_ffn_bk, L0_ffn_wv, L0_ffn_bv, L0_ffn_wo, L0_ffn_bo, L0_ffn_gate_w, L0_ffn_gate_b, L0_ffn_w1, L0_ffn_b1, L0_ffn_w2, L0_ffn_b2):

    def _L0_attn_ref(x, w_q, w_k, w_v, w_o):
        import jax, jax.numpy as jnp
        import numpy as np
        D_MODEL = 128
        N_HEADS = 16
        N_KV = 4
        HEAD_DIM = D_MODEL // N_HEADS
        SEQ = 256
        BATCH = 2
        CAP = 50.0
        EPS = 1e-05
        THETA = 10000.0

        def _rms_norm(x, eps=EPS):
            return x * jax.lax.rsqrt(jnp.mean(jnp.square(x), axis=-1, keepdims=True) + eps)

        def _rope_cos_sin(seq_len, head_dim, theta=THETA):
            inv_freq = 1.0 / theta ** (jnp.arange(0, head_dim, 2, dtype=jnp.float32) / head_dim)
            freqs = jnp.arange(seq_len, dtype=jnp.float32)[:, None] * inv_freq[None, :]
            return (jnp.cos(freqs)[None, :, None, :], jnp.sin(freqs)[None, :, None, :])

        def _apply_rope(x, cos, sin):
            d = x.shape[-1] // 2
            x1, x2 = (x[..., :d], x[..., d:])
            return jnp.concatenate([x1 * cos - x2 * sin, x2 * cos + x1 * sin], axis=-1).astype(x.dtype)
        B, S, _ = x.shape
        q = (x @ w_q).reshape(B, S, N_HEADS, HEAD_DIM)
        k = (x @ w_k).reshape(B, S, N_KV, HEAD_DIM)
        v = (x @ w_v).reshape(B, S, N_KV, HEAD_DIM)
        q = _rms_norm(q)
        k = _rms_norm(k)
        cos, sin = _rope_cos_sin(S, HEAD_DIM)
        q = _apply_rope(q, cos, sin)
        k = _apply_rope(k, cos, sin)
        rep = N_HEADS // N_KV
        k = jnp.repeat(k, rep, axis=2)
        v = jnp.repeat(v, rep, axis=2)
        scores = jnp.einsum('bqhd,bkhd->bhqk', q, k) / np.sqrt(HEAD_DIM).astype(np.float32)
        scores = jnp.tanh(scores.astype(jnp.float32) / CAP) * CAP
        causal = jnp.tril(jnp.ones((S, S), dtype=bool))
        scores = jnp.where(causal[None, None], scores, -jnp.inf)
        probs = jax.nn.softmax(scores, axis=-1)
        y = jnp.einsum('bhqk,bkhd->bqhd', probs, v).reshape(B, S, N_HEADS * HEAD_DIM)
        return y @ w_o

    def _L0_ffn_ref(x, ln1_g, ln1_b, ln2_g, ln2_b, wq, bq, wk, bk, wv, bv, wo, bo, gate_w, gate_b, w1, b1, w2, b2):
        import jax, jax.numpy as jnp
        import numpy as np
        B, S, H, NH, E, F = (4, 128, 128, 16, 8, 512)
        D = H // NH
        EPS = 1e-05

        def _layernorm(x, g, b):
            mu = jnp.mean(x, axis=-1, keepdims=True)
            var = jnp.var(x, axis=-1, keepdims=True)
            return (x - mu) * jax.lax.rsqrt(var + EPS) * g + b
        b, s, h = x.shape
        hn = _layernorm(x, ln1_g, ln1_b)
        q = (hn @ wq + bq).reshape(b, s, NH, D).transpose(0, 2, 1, 3)
        k = (hn @ wk + bk).reshape(b, s, NH, D).transpose(0, 2, 1, 3)
        v = (hn @ wv + bv).reshape(b, s, NH, D).transpose(0, 2, 1, 3)
        scores = jnp.einsum('bhqd,bhkd->bhqk', q, k) / jnp.sqrt(jnp.float32(D))
        attn = jax.nn.softmax(scores, axis=-1)
        o = jnp.einsum('bhqk,bhkd->bhqd', attn, v)
        o = o.transpose(0, 2, 1, 3).reshape(b, s, h)
        x = x + (o @ wo + bo)
        hn2 = _layernorm(x, ln2_g, ln2_b).reshape(-1, h)
        logits = hn2 @ gate_w + gate_b
        idx = jnp.argmax(logits, axis=-1)
        mid = jax.nn.relu(jnp.einsum('th,ehf->etf', hn2, w1) + b1[:, None, :])
        y = jnp.einsum('etf,efh->eth', mid, w2) + b2[:, None, :]
        moe = y[idx, jnp.arange(hn2.shape[0])]
        return x + moe.reshape(b, s, h)
    x = L0_attn_x
    x = _layernorm(x + _L0_attn_ref(x, L0_attn_w_q, L0_attn_w_k, L0_attn_w_v, L0_attn_w_o), axis=-1)
    x = _layernorm(x + _L0_ffn_ref(x, L0_ffn_ln1_g, L0_ffn_ln1_b, L0_ffn_ln2_g, L0_ffn_ln2_b, L0_ffn_wq, L0_ffn_bq, L0_ffn_wk, L0_ffn_bk, L0_ffn_wv, L0_ffn_bv, L0_ffn_wo, L0_ffn_bo, L0_ffn_gate_w, L0_ffn_gate_b, L0_ffn_w1, L0_ffn_b1, L0_ffn_w2, L0_ffn_b2), axis=-1)
    return x

_drawn_inputs = setup_inputs


def setup_inputs(seed=0):
    import zlib

    import numpy as np

    out = dict(_drawn_inputs(seed))
    spreads = {'L0_ffn_ln1_g': (1.0, 0.6),
     'L0_ffn_ln1_b': (0.0, 0.8),
     'L0_ffn_ln2_g': (1.0, 0.2),
     'L0_ffn_ln2_b': (0.0, 0.391),
     'L0_ffn_bq': (0.0, 0.8),
     'L0_ffn_bk': (0.0, 0.8),
     'L0_ffn_bv': (0.0, 0.491),
     'L0_ffn_bo': (0.0, 0.1),
     'L0_ffn_gate_b': (0.0, 0.1),
     'L0_ffn_b1': (0.0, 0.533),
     'L0_ffn_b2': (0.0, 0.1)}
    factors = {'L0_attn_w_q': 6.578,
     'L0_attn_w_k': 6.326,
     'L0_attn_w_v': 4.774,
     'L0_attn_w_o': 4.71,
     'L0_ffn_wq': 8.0,
     'L0_ffn_wk': 8.0,
     'L0_ffn_wv': 7.735,
     'L0_ffn_wo': 3.617}
    for name, (base, spread) in spreads.items():
        noise = np.random.default_rng([zlib.crc32(name.encode()), seed]).standard_normal(out[name].shape)
        drawn = base * np.exp(spread * noise) if base else spread * noise
        out[name] = jnp.asarray(drawn.astype(out[name].dtype))
    for name, factor in factors.items():
        out[name] = (out[name] * factor).astype(out[name].dtype)
    return out
```

```python
from contextlib import ExitStack

import numpy as np

import concourse.bass as bass
from concourse import mybir

ALU = mybir.AluOpType
ACT = mybir.ActivationFunctionType
F32 = mybir.dt.float32
F16 = mybir.dt.float16
I32 = mybir.dt.int32
X = mybir.AxisListType.X

P = 128
B, S, D = 16, 256, 128
NH, NKV, HD = 16, 4, 8
G = NH // 4
T = S // P
E, FF = 8, 512
FC = FF // P
CAP = 50.0
EPS = 1e-5
ISQ = 1.0 / np.sqrt(np.float32(HD))
MS = 64.0
HQ = T * NH
HK = T * NKV
HA = HQ + HK
TOK = B * S
REGION = TOK + P
SLOTS = -(-(TOK // P + E - 1) // 4) * 4
IDLE = SLOTS - TOK // P
ROWS = E * REGION + IDLE * P
ROW = 264
NCONST = dict(revexp=2 * E, base=E, ids=4, part=1, steps=E * (TOK // P), upto=E * E, slot=SLOTS * E,
              slotrow=SLOTS, half=HA)


def constants():
    inv = 1.0 / np.float32(10000.0) ** (np.arange(0, HD, 2, dtype=np.float32) / np.float32(HD))
    at = np.arange(S, dtype=np.float32)[:, None] * inv[None, :].astype(np.float32)
    cos, sin = np.cos(at).astype(np.float32), np.sin(at).astype(np.float32)
    cos = np.concatenate([cos, cos], 1).reshape(T, P, HD)
    sin = np.concatenate([-sin, sin], 1).reshape(T, P, HD)

    def spread(a):
        return np.concatenate([np.broadcast_to(a.transpose(1, 0, 2)[:, :, None, :], (P, T, h, HD)).reshape(P, -1)
                               for h in (NH, NKV)], 1)

    p = np.arange(P)[:, None]
    e = np.arange(E)
    rows = lambda a: np.broadcast_to(np.asarray(a, np.float32).reshape(1, -1), (P, np.size(a)))
    small = dict(
        revexp=rows(np.tile(E - e, 2)),
        base=rows(e * REGION),
        ids=(np.arange(2)[:, None] * S + np.arange(T)[None, :] * P).reshape(1, -1) + p - 2 * S,
        part=p,
        steps=rows(np.tile(np.arange(TOK // P) * P, (E, 1))),
        upto=rows(e[None, :] <= e[:, None]),
        slot=rows(np.repeat(np.arange(SLOTS), E)),
        slotrow=rows(np.arange(SLOTS) * P),
        half=rows(np.full(HA, -0.5)),
    )
    small = np.concatenate([np.asarray(small[k], np.float32).reshape(P, n) for k, n in NCONST.items()], 1)
    q = np.arange(P)
    return dict(
        c_rope=np.ascontiguousarray(np.concatenate([spread(cos), spread(sin)], 1), np.float32),
        c_square=np.concatenate([np.eye(P), p < q[None, :], np.ones((P, P))], 1).astype(np.float32),
        c_small=np.ascontiguousarray(small),
    )


class At:

    def __init__(self, scale, i, off):
        self.scale, self.i, self.off = scale, i, off

    def __add__(self, k):
        return At(self.scale, self.i, self.off + k)

    def __sub__(self, k):
        return self + (-k)

    def times(self, k, plus=0):
        return self.i * (self.scale * k) + (self.off * k + plus)

    @property
    def plain(self):
        return isinstance(self.i, int)


class Steps:

    def __init__(self, sem, names):
        self.sem, self.names = sem, names.split()

    def upto(self, n, name):
        return n.times(len(self.names), self.names.index(name) + 1)


def wait_value(eng, sem, v, apart):
    if not isinstance(v, int) or v > 0:
        if apart is not None and not isinstance(v, int):
            v = eng.to_reg(v)
            eng.wait_ge(apart, 1)
        eng.wait_ge(sem, v)


def wait(eng, steps, n, name, apart=None):
    wait_value(eng, steps.sem, steps.upto(n, name), apart)


def wait_turn(eng, sem, n, buffers, each, apart=None):
    wait_value(eng, sem, n.i * (n.scale // buffers * each) + (n.off // buffers + 1) * each, apart)


def post_ln_block(nc, x, w_q, w_k, w_v, w_o, ln1_g, ln1_b, ln2_g, ln2_b, wq, bq, wk, bk, wv, bv, wo, bo,
                  gate_w, gate_b, w1, b1, w2, b2, c_rope, c_square, c_small, out):
    with ExitStack() as ctx:
        def sb(name, shape, dt=F32):
            return ctx.enter_context(nc.sbuf_tensor(name, shape, dt))

        def psum(name, shape, dt=F32):
            return ctx.enter_context(nc.psum_tensor(name, shape, dt))

        def sem(name):
            return ctx.enter_context(nc.semaphore(name))

        def steps(name, names):
            return Steps(sem(name), names)

        routed = nc.dram_tensor("routed_rows", (ROWS, ROW), F32).ap()

        scores1 = psum("scores1", [P, 1024])
        scores2 = psum("scores2", [P, 1024])
        prep2 = psum("prep2", [P, 512])
        out1 = psum("out1", [P, 512])
        out2 = psum("out2", [P, 512])
        prep1 = psum("prep1", [P, 512])

        ident = sb("ident", [P, 3 * P])
        identh = sb("identh", [P, P], F16)
        rope = sb("rope", [P, 2, HA * HD])
        small = sb("small", [P, sum(NCONST.values())])
        w_qkv1 = sb("w_qkv1", [P, D + 2 * NKV * HD])
        w_out1 = sb("w_out1", [P, D])
        w_qkv2 = sb("w_qkv2", [P, 3 * D])
        w_out2 = sb("w_out2", [P, D])
        b_qkv2 = sb("b_qkv2", [P, 3 * D])
        b_out2 = sb("b_out2", [P, D])
        ln_cols = sb("ln_cols", [P, 4])
        w_gate = sb("w_gate", [P, E])
        b_gate = sb("b_gate", [P, T, E])
        w_up = sb("w_up", [P, E * FF])
        w_down = sb("w_down", [P, E * FF])
        b_up = sb("b_up", [P, E * FF])
        b_down = sb("b_down", [P, E * D])

        xs = sb("xs", [P, 2, T, D])
        xT = sb("xT", [P, S])
        qk1 = sb("qk1", [P, HA * HD])
        sq1 = sb("sq1", [P, HA * HD])
        ss1 = sb("ss1", [P, HA])
        ms1 = sb("ms1", [P, HA])
        rs1 = sb("rs1", [P, HA])
        rot1 = sb("rot1", [P, HA * HD])
        stack1 = sb("stack1", [P, HA, 32], F16)
        qs1 = sb("qs1", [P, 2, G, S], F16)
        km1 = sb("km1", [P, 2, 4, S], F16)
        v1 = sb("v1", [P, 2, T, NKV, 32])
        p1 = sb("p1", [P, 6, 1024])
        sums1 = sb("sums1", [P, G, S])
        rec1 = sb("rec1", [P, T, NH])
        o1 = sb("o1", [P, T, D])
        oT1 = sb("oT1", [P, S])
        r1 = sb("r1", [P, T, D])
        st1 = sb("st1", [P, T, 6])
        mv1 = sb("mv1", [P, T, 2])
        ve1 = sb("ve1", [P, T])
        rl1 = sb("rl1", [P, T])
        x1 = sb("x1", [P, 2, T, D])

        st2 = sb("st2", [P, T, 6])
        mv2 = sb("mv2", [P, T, 2])
        ve2 = sb("ve2", [P, T])
        rl2 = sb("rl2", [P, T])
        xh2 = sb("xh2", [P, T, D])
        hnT = sb("hnT", [P, S])
        qk2 = sb("qk2", [P, 2 * HQ * HD])
        stack2 = sb("stack2", [P, 2 * HQ, 32], F16)
        qs2 = sb("qs2", [P, 2, G, S], F16)
        kc2 = sb("kc2", [P, G, S], F16)
        km2 = sb("km2", [P, 2, G, 4, S], F16)
        v2 = sb("v2", [P, 2, T, NH, 32])
        mx2 = sb("mx2", [P, T, 4, G])
        nm2 = sb("nm2", [P, T, NH])
        mT2 = sb("mT2", [NH, S], F16)
        p2 = sb("p2", [P, 8, 1024])
        x1b = sb("x1b", [P, T, D])
        sums2 = sb("sums2", [P, G, S])
        rec2 = sb("rec2", [P, T, NH])
        o2 = sb("o2", [P, T, D])
        oT2 = sb("oT2", [P, S])
        r2 = sb("r2", [P, T, D])
        st3 = sb("st3", [P, T, 6])
        mv3 = sb("mv3", [P, T, 2])
        ve3 = sb("ve3", [P, T])
        rl3 = sb("rl3", [P, T])
        row = sb("row", [P, 2, T, ROW])
        h2T = sb("h2T", [P, S])

        lg = sb("lg", [P, T, E])
        top = sb("top", [P, T])
        eq = sb("eq", [P, T, E])
        rev = sb("rev", [P, T, E])
        top2 = sb("top2", [P, T])
        hot = sb("hot", [P, T, E])
        rb = sb("rb", [P, T, 2, E])
        place = sb("place", [P, T, E])
        posf = sb("posf", [P, T])
        pos = sb("pos", [P, 2, T], I32)
        cnt = sb("cnt", [P, E])
        ntile = sb("ntile", [P, E])
        csum = sb("csum", [P, E])
        jump = sb("jump", [P, E])
        slote = sb("slote", [P, SLOTS])
        slotr = sb("slotr", [P, SLOTS])
        slots = sb("slots", [P, 2, SLOTS], I32)
        padf = sb("padf", [P, E])
        padpos = sb("padpos", [P, E], I32)
        padrow = sb("padrow", [P, ROW])

        room = p1[:].rearrange("p u s -> p (u s)")
        taken = [0]

        def tile(n, width):
            o = taken[0]
            taken[0] += n * width
            return room[:, o:o + n * width].rearrange("p (n w) -> p n w", n=n)

        t_row, t_y = tile(4, ROW), tile(4, D)
        t_hT, t_z = tile(2, P), tile(2, D)
        t_mid, t_midT = tile(2, FF), tile(2, FF)
        full, below = tile(E, TOK // P), tile(E, E)
        passed, pjump = tile(SLOTS, E), tile(SLOTS, E)
        t_st = sb("t_st", [P, 2, 6])
        t_mv = sb("t_mv", [P, 2, 2])
        t_ve = sb("t_ve", [P, 2, 1])
        t_rs = sb("t_rs", [P, 2, 1])
        t_idx = sb("t_idx", [P, 4], I32)
        ps_hT = [scores1[:, 512 * j:512 * j + P] for j in range(2)]
        ps_up = [scores2[:, 512 * j:512 * j + FF] for j in range(2)]
        ps_mT = [prep1[:], prep2[:]]
        ps_down = [out1[:, 0:D], out2[:, 0:D]]

        o = 0
        const = {}
        for k, n in NCONST.items():
            const[k] = small[:, o:o + n]
            o += n
        eye, before, ones = (ident[:, j * P:(j + 1) * P] for j in range(3))
        prep1h, prep2h = prep1[:].bitcast(F16), prep2[:].bitcast(F16)

        consts_in, weights_in, experts_in = sem("consts_in"), sem("weights_in"), sem("experts_in")
        v_setup, p_setup, idle_rows = sem("v_setup"), sem("p_setup"), sem("idle_rows")
        x_in = [sem("x_in0"), sem("x_in1")]
        km_in = [sem("km_in0"), sem("km_in1")]
        m_in = [sem("m_in0"), sem("m_in1")]
        rows_out = [sem("rows_out0"), sem("rows_out1")]
        a_t = steps("a_t", "xT qkv qT kT")
        a_s = steps("a_s", "xT qs")
        a_v = steps("a_v", "in sq sum ms cos sin rot qn hi lo km")
        a_p = steps("a_p", "rms stack")
        b_t = steps("b_t", "sc0 sc1 sc2 sc3 sc4 sc5")
        b_s = steps("b_s", "tanh0 exp0 tanh1 exp1 tanh2 exp2 tanh3 exp3 tanh4 exp4 tanh5 exp5")
        b_p = steps("b_p", "mask0 mask1 mask2 mask3 mask4 mask5")
        c_t = steps("c_t", "pv0 pv1 ob0 ob1 oT y")
        c_s = steps("c_s", "pv0 pv1 oT")
        c_v = steps("c_v", "rec0 o0 rec1 o1 res st mv ve x1")
        c_p = steps("c_p", "rstd")
        MAXES = " ".join(f"max{j}" for j in range(4 * G))
        d_t = steps("d_t", f"xT qkv0 qkv1 qT kT {MAXES} mT")
        d_s = steps("d_s", "xT qs kc mT")
        d_v = steps("d_v", f"st mv ve xh qkv0 qkv1 hi lo {MAXES} nm")
        d_p = steps("d_p", "rstd stack")
        e_t = steps("e_t", " ".join(f"sc{j}" for j in range(8)))
        e_s = steps("e_s", " ".join(f"exp{j}" for j in range(8)))
        f_t = steps("f_t", "pv0 pv1 ob0 ob1 oT y hT gate rank")
        f_s = steps("f_s", "pv0 pv1 oT hT")
        f_v = steps("f_v", "rec0 o0 rec1 o1 x2 st mv sum ve xh id lg top eq rev top2 hot rb0 rb1 place posf pos")
        f_p = steps("f_p", "x1b rstd")
        r_v = steps("r_v", "padf pad cnt full ntile below csum jump passed e pjump r row e7 es")
        pads_out = sem("pads_out")
        tile_in = [sem(f"tile_in{j}") for j in range(4)]
        hT_t, up_t, mT_t, down_t = (steps(f"{k}_t", "x") for k in ("hT", "up", "mT", "down"))
        hT_s, relu_s = steps("hT_s", "x"), steps("relu_s", "x")
        up_v = steps("up_v", "x")
        z_v = steps("z_v", "z zb st mv ve idx")
        y_v = steps("y_v", "y")
        rstd_p = steps("rstd_p", "x")
        y_out = [sem(f"y_out{j}") for j in range(4)]

        x_d = x.rearrange("b s d -> (b s) d")
        out_d = out.rearrange("b s d -> (b s) d")

        LOADS = [(ident[:], c_square), (rope[:].rearrange("p a b -> p (a b)"), c_rope), (small[:], c_small)]
        WEIGHTS = [
            *[(w_qkv1[:, 32 * g:32 * g + 32].rearrange("p (i e) -> p i e", i=4),
               w_q.rearrange("d (i g e) -> d g i e", i=4, g=G)[:, g]) for g in range(G)],
            (w_qkv1[:, D:D + 32], w_k), (w_qkv1[:, D + 32:D + 64], w_v),
            (w_qkv2[:, 0:D], wq), (w_qkv2[:, D:2 * D], wk), (w_qkv2[:, 2 * D:3 * D], wv), (w_out2[:], wo),
            (w_gate[:], gate_w),
        ] + [(w_out1[32 * g + 8 * i:32 * g + 8 * i + 8, :], w_o[(4 * i + g) * 8:(4 * i + g) * 8 + 8, :])
             for g in range(G) for i in range(4)] + [
            (ln_cols[:, j:j + 1], v.rearrange("(d a) -> d a", a=1)) for j, v in enumerate((ln1_g, ln1_b, ln2_g, ln2_b))
        ] + [
            (dst, v.rearrange("(a d) -> a d", a=1).broadcast_to([P, v.shape[0]]))
            for dst, v in ((b_qkv2[:, 0:D], bq), (b_qkv2[:, D:2 * D], bk), (b_qkv2[:, 2 * D:3 * D], bv),
                           (b_out2[:], bo), (b_gate[:, 0, :], gate_b), (b_gate[:, 1, :], gate_b))
        ]
        EXPERTS = [
            (w_up[:].rearrange("d (e f) -> d e f", e=E), w1.rearrange("e d f -> d e f")),
            (w_down[:].rearrange("f (k h) -> f k h", h=D), w2.rearrange("e f h -> (e f) h").rearrange("(k f) h -> f k h", f=P)),
            (b_up[:], b1.rearrange("(a e) f -> a (e f)", a=1).broadcast_to([P, E * FF])),
            (b_down[:], b2.rearrange("(a e) h -> a (e h)", a=1).broadcast_to([P, E * D])),
        ]
        V_SETUP, P_SETUP = 8, 4

        XU, YP, XP = 2, 1, 3

        def maxes(a, b):
            return [(f"d_max{j}", YP) for j in range(a, b)]

        SEQ = [("a_load", XP), ("d_ln", YP), ("a_xT", XP), ("b_unit0", XU), ("e_unit0", 0), ("d_xh", YP),
               ("a_qkv", XP), ("d_xT", YP), ("b_unit1", XU), ("e_unit1", 0), ("d_qkv0", YP), ("d_qkv1", YP),
               ("a_split", XP), ("b_unit2", XU), ("e_unit2", 0), ("d_split", YP), ("b_unit3", XU),
               ("c_pv0", XU), ("e_unit3", 0), ("a_qT", XP), ("a_kT", XP), ("d_qT", YP), ("d_kT", YP),
               ("b_unit4", XU), ("e_unit4", 0), ("f_pv0", 0), *maxes(0, 4), ("b_unit5", XU), ("e_unit5", 0),
               *maxes(4, 8), ("c_pv1", XU), ("e_unit6", 0), *maxes(8, 12), ("c_ob0", XU), ("c_ob1", XU),
               ("e_unit7", 0), *maxes(12, 16), ("c_oT", XU), ("d_m", YP), ("f_pv1", 0), ("c_y", XU),
               ("f_ob0", 0), ("f_ob1", 0), ("f_oT", 0), ("f_y", 0), ("c_ln", XU), ("f_ln", 0), ("f_hT", 0),
               ("f_gate", 0), ("f_rank", 0), ("f_scatter", 0)]

        def pipeline(eng, parts):
            def iteration(n):
                for name, ahead in SEQ:
                    stem = name.rstrip("0123456789")
                    at = n + ahead
                    if stem in parts and (not at.plain or 0 <= at.off < B):
                        which = (int(name[len(stem):]),) if name != stem else ()
                        parts[stem](at, at.off % 2, *which)
            for k in range(-XP, 2):
                iteration(At(2, 0, k))
            with eng.Fori(1, B // 2 - 2) as i:
                for c in range(2):
                    iteration(At(2, i, c))
            for k in range(B - 4, B):
                iteration(At(2, 0, k))

        TILE_SEQ = [("hT", 1), ("up", 0), ("mT", -1), ("down", -2), ("y", -3)]

        def experts(eng, parts):
            def slot(n):
                for name, ahead in TILE_SEQ:
                    at = n + ahead
                    if name in parts and (not at.plain or 0 <= at.off < SLOTS):
                        parts[name](at, at.off % 4)
            for k in range(-1, 4):
                slot(At(4, 0, k))
            with eng.Fori(1, SLOTS // 4 - 1) as i:
                for c in range(4):
                    slot(At(4, i, c))
            for k in range(SLOTS - 4, SLOTS + 3):
                slot(At(4, 0, k))

        UNITS1 = [(0, (0,)), (0, (1,)), (1, (0, 1)), (0, (2,)), (0, (3,)), (1, (2, 3))]

        block = ctx.enter_context(nc.Block())

        @block.sync
        def _(sp):
            for dst, src in LOADS:
                sp.dma_start(dst, src).then_inc(consts_in, 16)

            def a_load(n, par):
                wait(sp, c_v, n - 2, "res", apart=v_setup)
                sp.dma_start(xs[:, par], x_d[bass.ds(n.times(S), S), :].rearrange("(t p) d -> p t d", p=P)
                             ).then_inc(x_in[par], 16)

            def d_kT(n, par):
                wait(sp, d_s, n, "kc", apart=v_setup)
                wait(sp, e_t, n - 2, "sc7", apart=v_setup)
                for i in range(4):
                    sp.dma_start(km2[32 * i:32 * i + 32, par, :, i, :], kc2[32 * i:32 * i + 32, :, :]
                                 ).then_inc(km_in[par], 16)

            def d_m(n, par):
                wait(sp, d_s, n, "mT", apart=v_setup)
                for i in range(4):
                    sp.dma_start(qs2[32 * i + 24:32 * i + 25, par, :, :], mT2[4 * i:4 * i + 4, :]
                                 ).then_inc(m_in[par], 16)

            for dst, src in WEIGHTS:
                sp.dma_start(dst, src).then_inc(weights_in, 16)
            for dst, src in EXPERTS:
                sp.dma_start(dst, src).then_inc(experts_in, 16)
            sp.wait_ge(v_setup, V_SETUP)
            sp.wait_ge(p_setup, P_SETUP)
            for j in range(IDLE):
                sp.dma_start(routed[E * REGION + j * P:E * REGION + (j + 1) * P, :], padrow[:, :]
                             ).then_inc(idle_rows, 16)

            pipeline(sp, dict(a_load=a_load, d_kT=d_kT, d_m=d_m))

            for j in range(2):
                sp.wait_ge(rows_out[j], 16 * T * B // 2)
            sp.wait_ge(pads_out, 16 * E)
            sp.wait_ge(idle_rows, 16 * IDLE)
            plan = At(1, 0, 0)
            wait(sp, r_v, plan, "es", apart=v_setup)

            def load_tile(s, q):
                wait(sp, z_v, s - 4, "idx", apart=v_setup)
                at = sp.value_load(slots[0:1, 1, bass.ds(s.times(1), 1)], min_val=0, max_val=ROWS - P)
                sp.dma_start(t_row[:, q, :], routed[bass.ds(at, P), :]).then_inc(tile_in[q], 16)

            for q in range(4):
                load_tile(At(4, 0, q), q)
            with sp.Fori(1, SLOTS // 4) as i:
                for q in range(4):
                    load_tile(At(4, i, q), q)
            for q in range(4):
                sp.wait_ge(y_out[q], 16 * (SLOTS // 4))

        @block.tensor
        def _(pe):
            pe.wait_ge(consts_in, 16 * len(LOADS))
            pe.wait_ge(weights_in, 16 * len(WEIGHTS))
            pe.wait_ge(v_setup, V_SETUP)
            pe.wait_ge(p_setup, P_SETUP)

            def a_xT(n, par):
                wait_turn(pe, x_in[par], n, 2, 16)
                wait(pe, a_v, n - 1, "km")
                for t in range(T):
                    mm = nc.tensor.transpose(prep1[:, t * P:(t + 1) * P], xs[:, par, t, :], eye)
                mm.then_inc(a_t.sem, 1)

            def a_qkv(n, par):
                wait(pe, a_s, n, "xT")
                for t in range(T):
                    mm = nc.tensor.matmul(prep1[:, t * 256:t * 256 + 192], xT[:, t * P:(t + 1) * P], w_qkv1[:],
                                          start=True, stop=True)
                mm.then_inc(a_t.sem, 1)

            def a_qT(n, par):
                wait(pe, a_p, n, "stack")
                for g in range(G):
                    for t in range(T):
                        h = t * NH + 4 * g
                        mm = nc.tensor.transpose(prep1h[:, g * S + t * P:g * S + t * P + P],
                                                 stack1[:, h:h + 4, :].rearrange("p h e -> p (h e)"), identh[:])
                mm.then_inc(a_t.sem, 1)

            def a_kT(n, par):
                wait(pe, a_s, n, "qs")
                for t in range(T):
                    h = HQ + 4 * t
                    mm = nc.tensor.transpose(prep1h[:, t * P:t * P + P],
                                             stack1[:, h:h + 4, :].rearrange("p h e -> p (h e)"), identh[:])
                mm.then_inc(a_t.sem, 1)

            def b_unit(n, par, u):
                if u == 0:
                    wait(pe, a_v, n, "km")
                    wait(pe, b_s, n - 1, "tanh5")
                else:
                    wait(pe, b_s, n, f"tanh{u - 1}")
                kt, groups = UNITS1[u]
                w = S // len(groups)
                for j, g in enumerate(groups):
                    for i in range(4):
                        mm = nc.tensor.matmul(scores1[:, (j * 4 + i) * w:(j * 4 + i + 1) * w],
                                              km1[:, par, i, kt * P:(kt + 1) * P], qs1[:, par, g, S - w:S],
                                              start=True, stop=True)
                mm.then_inc(b_t.sem, 1)

            def c_pv(n, par, j):
                wait(pe, b_p, n, f"mask{3 * j + 2}")
                if j == 0:
                    wait(pe, c_v, n - 1, "res")
                else:
                    wait(pe, c_s, n, "pv0")
                for k in range(2):
                    for i in range(4):
                        nc.tensor.matmul(out1[32 * i:32 * i + 32, k * S:(k + 1) * S], v1[:, par, 0, i, :],
                                         p1[:, 3 * j + k, i * S:(i + 1) * S], start=True, stop=False)
                    for i in range(4):
                        mm = nc.tensor.matmul(out1[32 * i:32 * i + 32, k * S + P:(k + 1) * S], v1[:, par, 1, i, :],
                                              p1[:, 3 * j + 2, (k * 4 + i) * P:(k * 4 + i + 1) * P],
                                              start=False, stop=True)
                mm.then_inc(c_t.sem, 1)

            def turn_back(out, sums, st, t):
                for g in range(G):
                    mm = nc.tensor.transpose(out[:, g * P:(g + 1) * P], sums[:, g, t * P:(t + 1) * P], eye)
                mm.then_inc(st.sem, 1)

            def c_ob(n, par, t):
                if t == 0:
                    wait(pe, c_s, n, "pv1")
                else:
                    wait(pe, c_v, n, "o0")
                turn_back(out1, sums1, c_t, t)

            def turn_o(out, o, st):
                for t in range(T):
                    mm = nc.tensor.transpose(out[:, t * P:(t + 1) * P], o[:, t, :], eye)
                mm.then_inc(st.sem, 1)

            def project(out, oT, w, st):
                for t in range(T):
                    mm = nc.tensor.matmul(out[:, t * D:(t + 1) * D], oT[:, t * P:(t + 1) * P], w[:],
                                          start=True, stop=True)
                mm.then_inc(st.sem, 1)

            def c_oT(n, par):
                wait(pe, c_v, n, "o1")
                turn_o(out1, o1, c_t)

            def c_y(n, par):
                wait(pe, c_s, n, "oT")
                project(out1, oT1, w_out1, c_t)

            def d_xT(n, par):
                wait(pe, d_v, n, "xh")
                wait(pe, d_s, n - 1, "mT")
                for t in range(T):
                    mm = nc.tensor.transpose(prep2[:, t * P:(t + 1) * P], xh2[:, t, :], eye)
                mm.then_inc(d_t.sem, 1)

            def d_qkv(n, par, t):
                if t == 0:
                    wait(pe, d_s, n, "xT")
                else:
                    wait(pe, d_v, n, "qkv0")
                nc.tensor.matmul(prep2[:, 0:3 * D], hnT[:, t * P:(t + 1) * P], w_qkv2[:],
                                 start=True, stop=True).then_inc(d_t.sem, 1)

            def turn_stack(first):
                for g in range(G):
                    for t in range(T):
                        h = first + t * NH + 4 * g
                        mm = nc.tensor.transpose(prep2h[:, g * S + t * P:g * S + t * P + P],
                                                 stack2[:, h:h + 4, :].rearrange("p h e -> p (h e)"), identh[:])
                mm.then_inc(d_t.sem, 1)

            def d_qT(n, par):
                wait(pe, d_p, n, "stack")
                turn_stack(0)

            def d_kT(n, par):
                wait(pe, d_s, n, "qs")
                turn_stack(HQ)

            def d_max(n, par, j):
                if j == 0:
                    wait_turn(pe, km_in[par], n, 2, 64)
                    wait(pe, d_s, n, "kc")
                else:
                    wait(pe, d_v, n, f"max{j - 1}")
                g, t, k = j // 4, j // 2 % 2, j % 2
                nc.tensor.matmul(prep2[:], qs2[:, par, g, t * P:(t + 1) * P],
                                 km2[:, par, g, 2 * k:2 * k + 2, :].rearrange("p i s -> p (i s)"),
                                 start=True, stop=True).then_inc(d_t.sem, 1)

            def d_m(n, par):
                wait(pe, d_v, n, "nm")
                for t in range(T):
                    mm = nc.tensor.transpose(prep2[0:NH, t * P:(t + 1) * P], nm2[:, t, :], eye)
                mm.then_inc(d_t.sem, 1)

            def e_unit(n, par, u):
                if u == 0:
                    wait_turn(pe, m_in[par], n, 2, 64)
                    wait(pe, e_s, n - 1, "exp7")
                else:
                    wait(pe, e_s, n, f"exp{u - 1}")
                g, kt = u // 2, u % 2
                for i in range(4):
                    mm = nc.tensor.matmul(scores2[:, i * S:(i + 1) * S], km2[:, par, g, i, kt * P:(kt + 1) * P],
                                          qs2[:, par, g, :], start=True, stop=True)
                mm.then_inc(e_t.sem, 1)

            def f_pv(n, par, j):
                wait(pe, e_s, n, f"exp{4 * j + 3}")
                if j == 0:
                    wait(pe, f_v, n - 1, "rb1")
                else:
                    wait(pe, f_s, n, "pv0")
                for k in range(2):
                    for kt in range(T):
                        for i in range(4):
                            mm = nc.tensor.matmul(out2[32 * i:32 * i + 32, k * S:(k + 1) * S],
                                                  v2[:, par, kt, 4 * (2 * j + k) + i, :],
                                                  p2[:, 4 * j + 2 * k + kt, i * S:(i + 1) * S],
                                                  start=(kt == 0), stop=(kt == T - 1))
                mm.then_inc(f_t.sem, 1)

            def f_ob(n, par, t):
                if t == 0:
                    wait(pe, f_s, n, "pv1")
                else:
                    wait(pe, f_v, n, "o0")
                turn_back(out2, sums2, f_t, t)

            def f_oT(n, par):
                wait(pe, f_v, n, "o1")
                turn_o(out2, o2, f_t)

            def f_y(n, par):
                wait(pe, f_s, n, "oT")
                project(out2, oT2, w_out2, f_t)

            def f_hT(n, par):
                wait(pe, f_v, n, "xh")
                for t in range(T):
                    mm = nc.tensor.transpose(out2[:, t * P:(t + 1) * P], row[:, par, t, 0:D], eye)
                mm.then_inc(f_t.sem, 1)

            def f_gate(n, par):
                wait(pe, f_s, n, "hT")
                for t in range(T):
                    mm = nc.tensor.matmul(out2[:, t * E:(t + 1) * E], h2T[:, t * P:(t + 1) * P], w_gate[:],
                                          start=True, stop=True)
                mm.then_inc(f_t.sem, 1)

            def f_rank(n, par):
                wait(pe, f_v, n, "hot")
                nc.tensor.matmul(out2[:, 0:T * E], before, hot[:].rearrange("p t e -> p (t e)"),
                                 start=True, stop=True)
                nc.tensor.matmul(out2[:, T * E:2 * T * E], ones, hot[:].rearrange("p t e -> p (t e)"),
                                 start=True, stop=True).then_inc(f_t.sem, 1)

            pipeline(pe, dict(a_xT=a_xT, a_qkv=a_qkv, a_qT=a_qT, a_kT=a_kT, b_unit=b_unit, c_pv=c_pv, c_ob=c_ob,
                              c_oT=c_oT, c_y=c_y, d_xT=d_xT, d_qkv=d_qkv, d_qT=d_qT, d_kT=d_kT, d_max=d_max,
                              d_m=d_m, e_unit=e_unit, f_pv=f_pv, f_ob=f_ob, f_oT=f_oT, f_y=f_y, f_hT=f_hT,
                              f_gate=f_gate, f_rank=f_rank))

            pe.wait_ge(experts_in, 16 * len(EXPERTS))
            wait(pe, r_v, At(1, 0, 0), "es")

            def expert(s):
                return pe.value_load(slots[0:1, 0, bass.ds(s.times(1), 1)], min_val=0, max_val=E - 1)

            def hT(s, q):
                wait_turn(pe, tile_in[q], s, 4, 16)
                wait(pe, hT_s, s - 2, "x")
                nc.tensor.transpose(ps_hT[q % 2], t_row[:, q, 0:D], eye).then_inc(hT_t.sem, 1)

            def up(s, q):
                e = expert(s)
                wait(pe, hT_s, s, "x")
                wait(pe, up_v, s - 2, "x")
                nc.tensor.matmul(ps_up[q % 2], t_hT[:, q % 2, :], w_up[:, bass.ds(e * FF, FF)],
                                 start=True, stop=True).then_inc(up_t.sem, 1)

            def mT(s, q):
                wait(pe, up_v, s, "x")
                wait(pe, relu_s, s - 2, "x")
                for c in range(FC):
                    mm = nc.tensor.transpose(ps_mT[q % 2][:, c * P:(c + 1) * P],
                                             t_mid[:, q % 2, c * P:(c + 1) * P], eye)
                mm.then_inc(mT_t.sem, 1)

            def down(s, q):
                e = expert(s)
                wait(pe, relu_s, s, "x")
                wait(pe, z_v, s - 2, "z")
                for c in range(FC):
                    mm = nc.tensor.matmul(ps_down[q % 2], t_midT[:, q % 2, c * P:(c + 1) * P],
                                          w_down[:, bass.ds(e * FF + c * P, D)], start=(c == 0), stop=(c == FC - 1))
                mm.then_inc(down_t.sem, 1)

            experts(pe, dict(hT=hT, up=up, mT=mT, down=down))

        @block.scalar
        def _(act):
            act.wait_ge(weights_in, 16 * len(WEIGHTS))

            def a_xT(n, par):
                wait(act, a_t, n, "xT")
                nc.scalar.copy(xT[:], prep1[:, 0:S]).then_inc(a_s.sem, 1)

            def a_qT(n, par):
                wait(act, a_t, n, "qT")
                wait(act, b_t, n - 2, "sc5")
                nc.scalar.copy(qs1[:, par].rearrange("p g s -> p (g s)"), prep1h).then_inc(a_s.sem, 1)

            def b_unit(n, par, u):
                wait(act, b_t, n, f"sc{u}")
                wait(act, c_t, n - 1, f"pv{u // 3}")
                nc.scalar.activation(p1[:, u], scores1[:], ACT.Tanh, scale=float(ISQ / CAP)).then_inc(b_s.sem, 1)
                wait(act, b_s, n, f"tanh{u}")
                nc.scalar.activation(p1[:, u], p1[:, u], ACT.Exp, scale=CAP).then_inc(b_s.sem, 1)

            def c_pv(n, par, j):
                wait(act, c_t, n, f"pv{j}")
                wait(act, c_t, n - 1, "ob1")
                nc.scalar.copy(sums1[:, 2 * j:2 * j + 2, :].rearrange("p g s -> p (g s)"), out1[:]
                               ).then_inc(c_s.sem, 1)

            def c_oT(n, par):
                wait(act, c_t, n, "oT")
                nc.scalar.copy(oT1[:], out1[:, 0:S]).then_inc(c_s.sem, 1)

            def d_xT(n, par):
                wait(act, d_t, n, "xT")
                nc.scalar.activation(hnT[:], prep2[:, 0:S], ACT.Identity, scale=ln_cols[:, 0:1],
                                     bias=ln_cols[:, 1:2]).then_inc(d_s.sem, 1)

            def d_qT(n, par):
                wait(act, d_t, n, "qT")
                wait(act, e_t, n - 2, "sc7")
                nc.scalar.copy(qs2[:, par].rearrange("p g s -> p (g s)"), prep2h).then_inc(d_s.sem, 1)

            def d_kT(n, par):
                wait(act, d_t, n, "kT")
                wait_turn(act, km_in[1 - par], n - 1, 2, 64)
                nc.scalar.copy(kc2[:].rearrange("p g s -> p (g s)"), prep2h).then_inc(d_s.sem, 1)

            def d_m(n, par):
                wait(act, d_t, n, "mT")
                wait_turn(act, m_in[1 - par], n - 1, 2, 64)
                nc.scalar.copy(mT2[:], prep2[0:NH, 0:S]).then_inc(d_s.sem, 1)

            def e_unit(n, par, u):
                wait(act, e_t, n, f"sc{u}")
                wait(act, f_t, n - 1, f"pv{u // 4}")
                nc.scalar.activation(p2[:, u], scores2[:], ACT.Exp, scale=float(ISQ)).then_inc(e_s.sem, 1)

            def f_pv(n, par, j):
                wait(act, f_t, n, f"pv{j}")
                wait(act, f_t, n - 1, "ob1")
                nc.scalar.copy(sums2[:, 2 * j:2 * j + 2, :].rearrange("p g s -> p (g s)"), out2[:]
                               ).then_inc(f_s.sem, 1)

            def f_oT(n, par):
                wait(act, f_t, n, "oT")
                nc.scalar.copy(oT2[:], out2[:, 0:S]).then_inc(f_s.sem, 1)

            def f_hT(n, par):
                wait(act, f_t, n, "hT")
                nc.scalar.activation(h2T[:], out2[:, 0:S], ACT.Identity, scale=ln_cols[:, 2:3],
                                     bias=ln_cols[:, 3:4]).then_inc(f_s.sem, 1)

            pipeline(act, dict(a_xT=a_xT, a_qT=a_qT, b_unit=b_unit, c_pv=c_pv, c_oT=c_oT, d_xT=d_xT, d_qT=d_qT,
                               d_kT=d_kT, d_m=d_m, e_unit=e_unit, f_pv=f_pv, f_oT=f_oT, f_hT=f_hT))

            def hT(s, q):
                wait(act, hT_t, s, "x")
                wait(act, up_t, s - 2, "x")
                nc.scalar.activation(t_hT[:, q % 2, :], ps_hT[q % 2], ACT.Identity, scale=ln_cols[:, 2:3],
                                     bias=ln_cols[:, 3:4]).then_inc(hT_s.sem, 1)

            def mT(s, q):
                wait(act, mT_t, s, "x")
                wait(act, down_t, s - 2, "x")
                nc.scalar.activation(t_midT[:, q % 2, :], ps_mT[q % 2], ACT.Relu).then_inc(relu_s.sem, 1)

            experts(act, dict(hT=hT, mT=mT))

        @block.vector
        def _(dve):
            dve.wait_ge(consts_in, 16 * len(LOADS))
            nc.vector.tensor_copy(identh[:], eye).then_inc(v_setup, 1)
            nc.vector.tensor_copy(rb[:, 1, 1, :], const["base"]).then_inc(v_setup, 1)
            nc.vector.memset(row[:, :, :, D * 2 + 1:], 0.0).then_inc(v_setup, 1)
            nc.vector.tensor_copy(row[:, :, :, 2 * D:2 * D + 1],
                                  const["ids"].rearrange("p (b t a) -> p b t a", b=2, a=1)).then_inc(v_setup, 1)
            nc.vector.memset(padrow[:], 0.0).then_inc(v_setup, 1)
            dve.wait_ge(v_setup, 5)
            nc.vector.memset(padrow[:, 2 * D:2 * D + 1], float(TOK)).then_inc(v_setup, 1)
            nc.vector.memset(km2[:].rearrange("p a g i s -> p (a g i s)").bitcast(F32), 0.0).then_inc(v_setup, 1)
            nc.vector.memset(v2[:], 1.0).then_inc(v_setup, 1)
            dve.wait_ge(p_setup, P_SETUP)
            dve.wait_ge(v_setup, V_SETUP)
            dve.wait_ge(weights_in, 16 * len(WEIGHTS))
            cosines, sines = rope[:, 0, :], rope[:, 1, :].rearrange("p (h a e) -> p h a e", a=2, e=HD // 2)

            def a_qkv(n, par):
                wait(dve, a_t, n, "qkv")
                wait(dve, c_t, n - 2, "pv1")
                got = prep1[:].rearrange("p (t e) -> p t e", t=T)
                nc.vector.tensor_copy(qk1[:, 0:T * D].rearrange("p (t e) -> p t e", t=T), got[:, :, 0:D])
                nc.vector.tensor_copy(qk1[:, T * D:].rearrange("p (t e) -> p t e", t=T), got[:, :, D:D + 32])
                nc.vector.tensor_copy(v1[:, par, :, :, 0:HD],
                                      got[:, :, D + 32:D + 64].rearrange("p t (i e) -> p t i e", i=NKV)
                                      ).then_inc(a_v.sem, 1)
                wait(dve, a_v, n, "in")
                nc.vector.tensor_tensor(sq1[:], qk1[:], qk1[:], ALU.mult).then_inc(a_v.sem, 1)
                wait(dve, a_v, n, "sq")
                nc.vector.tensor_reduce(ss1[:], sq1[:].rearrange("p (h e) -> p h e", e=HD), X, ALU.add
                                        ).then_inc(a_v.sem, 1)
                wait(dve, a_v, n, "sum")
                nc.vector.tensor_scalar(ms1[:], ss1[:], 1.0 / HD, EPS, ALU.mult, ALU.add).then_inc(a_v.sem, 1)
                nc.vector.tensor_tensor(rot1[:], qk1[:], cosines, ALU.mult).then_inc(a_v.sem, 1)
                q4 = qk1[:].rearrange("p (h a e) -> p h a e", a=2, e=HD // 2)
                s4 = sq1[:].rearrange("p (h a e) -> p h a e", a=2, e=HD // 2)
                nc.vector.tensor_tensor(s4[:, :, 0, :], q4[:, :, 1, :], sines[:, :, 0, :], ALU.mult)
                nc.vector.tensor_tensor(s4[:, :, 1, :], q4[:, :, 0, :], sines[:, :, 1, :], ALU.mult
                                        ).then_inc(a_v.sem, 1)
                wait(dve, a_v, n, "sin")
                nc.vector.tensor_tensor(rot1[:], rot1[:], sq1[:], ALU.add).then_inc(a_v.sem, 1)

            def a_split(n, par):
                wait(dve, a_v, n, "rot")
                wait(dve, a_p, n, "rms")
                nc.vector.tensor_tensor(qk1[:].rearrange("p (h e) -> p h e", e=HD),
                                        rot1[:].rearrange("p (h e) -> p h e", e=HD),
                                        rs1[:].rearrange("p (h a) -> p h a", a=1).broadcast_to([P, HA, HD]),
                                        ALU.mult).then_inc(a_v.sem, 1)
                wait(dve, a_v, n, "qn")
                wait(dve, a_t, n - 1, "kT")
                q3 = qk1[:].rearrange("p (h e) -> p h e", e=HD)
                nc.vector.tensor_copy(stack1[:, :, 0:HD], q3).then_inc(a_v.sem, 1)
                wait(dve, a_v, n, "hi")
                nc.vector.tensor_tensor(stack1[:, :, 3 * HD:], q3, stack1[:, :, 0:HD], ALU.subtract
                                        ).then_inc(a_v.sem, 1)

            def a_kT(n, par):
                wait(dve, a_t, n, "kT")
                wait(dve, b_t, n - 2, "sc5")
                for i in range(4):
                    last = nc.vector.tensor_copy(km1[32 * i:32 * i + 32, par, i, :], prep1h[32 * i:32 * i + 32, 0:S])
                last.then_inc(a_v.sem, 1)

            def normalise(out, rec, o, n, t, st):
                heads = out[:].rearrange("p (h e) -> p h e", h=NH)
                nc.vector.reciprocal(rec[:, t, :].rearrange("p (h a) -> p h a", a=1), heads[:, :, HD:HD + 1]
                                     ).then_inc(st.sem, 1)
                wait(dve, st, n, f"rec{t}")
                nc.vector.tensor_tensor(o[:, t, :].rearrange("p (h e) -> p h e", h=NH), heads[:, :, 0:HD],
                                        rec[:, t, :].rearrange("p (h a) -> p h a", a=1).broadcast_to([P, NH, HD]),
                                        ALU.mult).then_inc(st.sem, 1)

            def c_ob(n, par, t):
                wait(dve, c_t, n, f"ob{t}")
                normalise(out1, rec1, o1, n, t, c_v)

            def moments(r, st_, mv, n, steps_):
                for t in range(T):
                    last = nc.vector.bn_stats(st_[:, t, :], r[:, t, :])
                last.then_inc(steps_.sem, 1)
                wait(dve, steps_, n, "st", apart=v_setup)
                for t in range(T):
                    last = nc.vector.bn_aggr(mv[:, t, :], st_[:, t, :])
                last.then_inc(steps_.sem, 1)

            def c_y(n, par):
                wait(dve, c_t, n, "y")
                nc.vector.tensor_tensor(r1[:], out1[:, 0:T * D].rearrange("p (t d) -> p t d", t=T), xs[:, par],
                                        ALU.add).then_inc(c_v.sem, 1)
                wait(dve, c_v, n, "res")
                moments(r1, st1, mv1, n, c_v)
                wait(dve, c_v, n, "mv")
                nc.vector.tensor_scalar(ve1[:], mv1[:, :, 1], EPS, None, ALU.add).then_inc(c_v.sem, 1)

            def norm(dst, src, mv, rl):
                for t in range(T):
                    last = nc.vector.tensor_scalar(dst(t), src[:, t, :], mv[:, t, 0:1], rl[:, t:t + 1],
                                                   ALU.subtract, ALU.mult)
                return last

            def c_ln(n, par):
                wait(dve, c_p, n, "rstd")
                wait(dve, f_v, n - 2, "sum")
                wait(dve, f_p, n - 2, "x1b")
                norm(lambda t: x1[:, par, t, :], r1, mv1, rl1).then_inc(c_v.sem, 1)

            def d_ln(n, par):
                wait(dve, c_v, n, "x1")
                moments(x1[:, par], st2, mv2, n, d_v)
                wait(dve, d_v, n, "mv")
                nc.vector.tensor_scalar(ve2[:], mv2[:, :, 1], EPS, None, ALU.add).then_inc(d_v.sem, 1)

            def d_xh(n, par):
                wait(dve, d_p, n, "rstd")
                wait(dve, d_t, n - 1, "xT")
                norm(lambda t: xh2[:, t, :], x1[:, par], mv2, rl2).then_inc(d_v.sem, 1)

            def d_qkv(n, par, t):
                wait(dve, d_t, n, f"qkv{t}")
                wait(dve, f_t, n - 2, "pv1")
                nc.vector.tensor_tensor(
                    qk2[:].rearrange("p (a t x) -> p a t x", a=2, t=T)[:, :, t, :],
                    prep2[:, 0:2 * D].rearrange("p (a x) -> p a x", a=2),
                    b_qkv2[:, 0:2 * D].rearrange("p (a x) -> p a x", a=2), ALU.add)
                nc.vector.tensor_tensor(
                    v2[:, par, t, :, 0:HD], prep2[:, 2 * D:3 * D].rearrange("p (h e) -> p h e", h=NH),
                    b_qkv2[:, 2 * D:3 * D].rearrange("p (h e) -> p h e", h=NH), ALU.add).then_inc(d_v.sem, 1)

            def d_split(n, par):
                wait(dve, d_v, n, "qkv1")
                wait(dve, d_t, n - 1, "kT")
                q3 = qk2[:].rearrange("p (h e) -> p h e", e=HD)
                nc.vector.tensor_copy(stack2[:, :, 0:HD], q3).then_inc(d_v.sem, 1)
                wait(dve, d_v, n, "hi")
                nc.vector.tensor_tensor(stack2[:, 0:HQ, 2 * HD:3 * HD], q3[:, 0:HQ], stack2[:, 0:HQ, 0:HD],
                                        ALU.subtract)
                nc.vector.tensor_tensor(stack2[:, HQ:, HD:2 * HD], q3[:, HQ:], stack2[:, HQ:, 0:HD],
                                        ALU.subtract).then_inc(d_v.sem, 1)

            def d_max(n, par, j):
                wait(dve, d_t, n, f"max{j}")
                g, t, k = j // 4, j // 2 % 2, j % 2
                nc.vector.tensor_reduce(mx2[:, t, 2 * k:2 * k + 2, g], prep2[:].rearrange("p (i s) -> p i s", i=2),
                                        X, ALU.max).then_inc(d_v.sem, 1)

            def d_m(n, par):
                wait(dve, d_v, n, "max15")
                wait(dve, d_t, n - 1, "mT")
                nc.vector.tensor_scalar(nm2[:].rearrange("p t h -> p (t h)"),
                                        mx2[:].rearrange("p t i g -> p (t i g)"), -1.0 / MS, -65504.0,
                                        ALU.mult, ALU.max).then_inc(d_v.sem, 1)

            def f_ob(n, par, t):
                wait(dve, f_t, n, f"ob{t}")
                normalise(out2, rec2, o2, n, t, f_v)

            def f_y(n, par):
                wait(dve, f_t, n, "y")
                wait(dve, f_p, n, "x1b")
                nc.vector.tensor_tensor(r2[:], out2[:, 0:T * D].rearrange("p (t d) -> p t d", t=T), x1b[:],
                                        ALU.add).then_inc(f_v.sem, 1)
                wait(dve, f_v, n, "x2")
                moments(r2, st3, mv3, n, f_v)
                wait_turn(dve, rows_out[par], n - 2, 2, 16 * T)
                nc.vector.tensor_tensor(row[:, par, :, D:2 * D], x1[:, par], r2[:], ALU.add).then_inc(f_v.sem, 1)
                wait(dve, f_v, n, "mv")
                nc.vector.tensor_scalar(ve3[:], mv3[:, :, 1], EPS, None, ALU.add).then_inc(f_v.sem, 1)

            def f_ln(n, par):
                wait(dve, f_p, n, "rstd")
                norm(lambda t: row[:, par, t, 0:D], r2, mv3, rl3).then_inc(f_v.sem, 1)
                nc.vector.tensor_scalar(row[:, par, :, 2 * D], row[:, par, :, 2 * D], float(2 * S), None, ALU.add
                                        ).then_inc(f_v.sem, 1)

            def f_gate(n, par):
                def spread(a):
                    return a[:].rearrange("p (t a) -> p t a", a=1).broadcast_to([P, T, E])
                wait(dve, f_t, n, "gate")
                nc.vector.tensor_tensor(lg[:], out2[:, 0:T * E].rearrange("p (t e) -> p t e", t=T), b_gate[:],
                                        ALU.add).then_inc(f_v.sem, 1)
                wait(dve, f_v, n, "lg")
                nc.vector.tensor_reduce(top[:], lg[:], X, ALU.max).then_inc(f_v.sem, 1)
                wait(dve, f_v, n, "top")
                nc.vector.tensor_tensor(eq[:], lg[:], spread(top), ALU.is_ge).then_inc(f_v.sem, 1)
                wait(dve, f_v, n, "eq")
                nc.vector.tensor_tensor(rev[:], eq[:], const["revexp"].rearrange("p (t e) -> p t e", t=T),
                                        ALU.mult).then_inc(f_v.sem, 1)
                wait(dve, f_v, n, "rev")
                nc.vector.tensor_reduce(top2[:], rev[:], X, ALU.max).then_inc(f_v.sem, 1)
                wait(dve, f_v, n, "top2")
                nc.vector.tensor_tensor(hot[:], rev[:], spread(top2), ALU.is_ge).then_inc(f_v.sem, 1)

            def f_rank(n, par):
                wait(dve, f_t, n, "rank")
                for t in range(T):
                    if t:
                        wait(dve, f_v, n, "rb0")
                    nc.vector.tensor_tensor(
                        rb[:, t], out2[:, 0:2 * T * E].rearrange("p (k t e) -> p k t e", k=2, t=T)[:, :, t, :],
                        rb[:, 1 - t, 1, :].rearrange("p (a e) -> p a e", a=1).broadcast_to([P, 2, E]),
                        ALU.add).then_inc(f_v.sem, 1)
                wait(dve, f_v, n, "rb1")
                nc.vector.tensor_tensor(place[:], rb[:, :, 0, :], hot[:], ALU.mult).then_inc(f_v.sem, 1)
                wait(dve, f_v, n, "place")
                nc.vector.tensor_reduce(posf[:], place[:], X, ALU.add).then_inc(f_v.sem, 1)
                wait(dve, f_v, n, "posf")
                nc.vector.tensor_copy(pos[:, par, :], posf[:]).then_inc(f_v.sem, 1)

            pipeline(dve, dict(a_qkv=a_qkv, a_split=a_split, a_kT=a_kT, c_ob=c_ob, c_y=c_y, c_ln=c_ln, d_ln=d_ln,
                               d_xh=d_xh, d_qkv=d_qkv, d_split=d_split, d_max=d_max, d_m=d_m, f_ob=f_ob, f_y=f_y,
                               f_ln=f_ln, f_gate=f_gate, f_rank=f_rank))

            plan = At(1, 0, 0)
            last_rows = rb[:, 1, 1, :]

            def over(a, k):
                return a.rearrange("p (n a) -> p n a", a=1).broadcast_to([P, a.shape[1], k])

            def under(a, k):
                return a.rearrange("p (a n) -> p a n", a=1).broadcast_to([P, k, a.shape[1]])

            def done(ins, name):
                ins.then_inc(r_v.sem, 1)
                wait(dve, r_v, plan, name)

            wait(dve, f_v, At(1, 0, B - 1), "pos")
            done(nc.vector.tensor_tensor(padf[:], last_rows, const["part"].broadcast_to([P, E]), ALU.add), "padf")
            done(nc.vector.tensor_copy(padpos[:], padf[:]), "pad")
            done(nc.vector.tensor_tensor(cnt[:], last_rows, const["base"], ALU.subtract), "cnt")
            done(nc.vector.tensor_tensor(full[:], over(cnt[:], TOK // P),
                                         const["steps"].rearrange("p (e k) -> p e k", e=E), ALU.is_gt), "full")
            done(nc.vector.tensor_reduce(ntile[:], full[:], X, ALU.add), "ntile")
            done(nc.vector.tensor_tensor(below[:], const["upto"].rearrange("p (e k) -> p e k", e=E),
                                         under(ntile[:], E), ALU.mult), "below")
            done(nc.vector.tensor_reduce(csum[:], below[:], X, ALU.add), "csum")
            done(nc.vector.tensor_scalar(jump[:], ntile[:], float(-P), float(REGION), ALU.mult, ALU.add), "jump")
            done(nc.vector.tensor_tensor(passed[:], const["slot"].rearrange("p (s e) -> p s e", e=E),
                                         under(csum[:], SLOTS), ALU.is_ge), "passed")
            done(nc.vector.tensor_reduce(slote[:], passed[:], X, ALU.add), "e")
            done(nc.vector.tensor_tensor(pjump[:], passed[:], under(jump[:], SLOTS), ALU.mult), "pjump")
            done(nc.vector.tensor_reduce(slotr[:], pjump[:], X, ALU.add), "r")
            done(nc.vector.tensor_tensor(slots[:, 1, :], slotr[:], const["slotrow"], ALU.add), "row")
            done(nc.vector.tensor_scalar(slote[:], slote[:], float(E - 1), None, ALU.min), "e7")
            done(nc.vector.tensor_copy(slots[:, 0, :], slote[:]), "es")

            dve.wait_ge(experts_in, 16 * len(EXPERTS))

            def expert(s):
                return dve.value_load(slots[0:1, 0, bass.ds(s.times(1), 1)], min_val=0, max_val=E - 1)

            def up(s, q):
                e = expert(s)
                wait(dve, up_t, s, "x")
                wait(dve, mT_t, s - 2, "x")
                nc.vector.tensor_tensor(t_mid[:, q % 2, :], ps_up[q % 2], b_up[:, bass.ds(e * FF, FF)], ALU.add
                                        ).then_inc(up_v.sem, 1)

            def down(s, q):
                h = q % 2
                e = expert(s)
                wait(dve, down_t, s, "x")
                wait(dve, y_v, s - 2, "y")
                nc.vector.tensor_tensor(t_z[:, h, :], ps_down[h], t_row[:, q, D:2 * D], ALU.add).then_inc(z_v.sem, 1)
                wait(dve, z_v, s, "z")
                nc.vector.tensor_tensor(t_z[:, h, :], t_z[:, h, :], b_down[:, bass.ds(e * D, D)], ALU.add
                                        ).then_inc(z_v.sem, 1)
                wait(dve, z_v, s, "zb")
                nc.vector.bn_stats(t_st[:, h, :], t_z[:, h, :]).then_inc(z_v.sem, 1)
                wait(dve, z_v, s, "st", apart=v_setup)
                nc.vector.bn_aggr(t_mv[:, h, :], t_st[:, h, :]).then_inc(z_v.sem, 1)
                wait(dve, z_v, s, "mv")
                nc.vector.tensor_scalar(t_ve[:, h, :], t_mv[:, h, 1:2], EPS, None, ALU.add).then_inc(z_v.sem, 1)
                wait_turn(dve, y_out[q], s - 4, 4, 16)
                nc.vector.tensor_copy(t_idx[:, q:q + 1], t_row[:, q, 2 * D:2 * D + 1]).then_inc(z_v.sem, 1)

            def y(s, q):
                h = q % 2
                wait(dve, rstd_p, s, "x")
                nc.vector.tensor_scalar(t_y[:, q, :], t_z[:, h, :], t_mv[:, h, 0:1], t_rs[:, h, :],
                                        ALU.subtract, ALU.mult).then_inc(y_v.sem, 1)

            experts(dve, dict(up=up, down=down, y=y))

        @block.gpsimd
        def _(pool):
            nc.gpsimd.memset(km1[:].rearrange("p a i s -> p (a i s)").bitcast(F32), 0.0).then_inc(p_setup, 1)
            nc.gpsimd.memset(v1[:], 1.0).then_inc(p_setup, 1)
            nc.gpsimd.memset(stack2[:, :, 3 * HD:], 0.0).then_inc(p_setup, 1)
            pool.wait_ge(p_setup, 3)
            nc.gpsimd.memset(stack2[:, HQ:, 3 * HD:3 * HD + 1], MS).then_inc(p_setup, 1)
            pool.wait_ge(consts_in, 16 * len(LOADS))
            pool.wait_ge(weights_in, 16 * len(WEIGHTS))
            pool.wait_ge(v_setup, V_SETUP)
            pool.wait_ge(p_setup, P_SETUP)
            half = const["half"]

            def a_qkv(n, par):
                wait(pool, a_v, n, "ms", apart=v_setup)
                nc.gpsimd.tensor_tensor(rs1[:], ms1[:], half, ALU.pow).then_inc(a_p.sem, 1)

            def move(dst, src):
                return nc.gpsimd.tensor_scalar(dst, src, 1.0, None, ALU.mult)

            def a_split(n, par):
                wait(pool, a_v, n, "lo", apart=v_setup)
                hi, lo = stack1[:, :, 0:HD], stack1[:, :, 3 * HD:]
                move(stack1[:, 0:HQ, HD:2 * HD], hi[:, 0:HQ])
                move(stack1[:, 0:HQ, 2 * HD:3 * HD], lo[:, 0:HQ])
                move(stack1[:, HQ:, HD:2 * HD], lo[:, HQ:])
                move(stack1[:, HQ:, 2 * HD:3 * HD], hi[:, HQ:]).then_inc(a_p.sem, 1)

            def b_unit(n, par, u):
                wait(pool, b_s, n, f"exp{u}", apart=v_setup)
                if UNITS1[u][0] == 0:
                    w = p1[:, u].rearrange("p (i s) -> p i s", i=4)[:, :, 0:P]
                else:
                    w = p1[:, u].rearrange("p (i s) -> p i s", i=8)
                nc.gpsimd.affine_select(out=w, in_=w, compare_op=ALU.is_ge, fill=0.0, base=0,
                                        pattern=[[0, w.shape[1]], [1, P]], channel_multiplier=-1).then_inc(b_p.sem, 1)

            def c_y(n, par):
                wait(pool, c_v, n, "ve", apart=v_setup)
                nc.gpsimd.tensor_tensor(rl1[:], ve1[:], half[:, 0:T], ALU.pow).then_inc(c_p.sem, 1)

            def d_ln(n, par):
                wait(pool, d_v, n, "ve", apart=v_setup)
                nc.gpsimd.tensor_tensor(rl2[:], ve2[:], half[:, 0:T], ALU.pow).then_inc(d_p.sem, 1)

            def d_split(n, par):
                wait(pool, d_v, n, "lo", apart=v_setup)
                move(stack2[:, 0:HQ, HD:2 * HD], stack2[:, 0:HQ, 0:HD])
                move(stack2[:, HQ:, 2 * HD:3 * HD], stack2[:, HQ:, 0:HD]).then_inc(d_p.sem, 1)

            def f_pv(n, par, j):
                if j == 0:
                    wait(pool, f_v, n - 1, "x2", apart=v_setup)
                    nc.gpsimd.tensor_tensor(x1b[:], x1[:, par],
                                            b_out2[:].rearrange("p (a d) -> p a d", a=1).broadcast_to([P, T, D]),
                                            ALU.add).then_inc(f_p.sem, 1)

            def f_y(n, par):
                wait(pool, f_v, n, "ve", apart=v_setup)
                nc.gpsimd.tensor_tensor(rl3[:], ve3[:], half[:, 0:T], ALU.pow).then_inc(f_p.sem, 1)

            def f_scatter(n, par):
                wait(pool, f_v, n, "pos", apart=v_setup)
                for t in range(T):
                    pool.indirect_dma_start(
                        out=routed, out_offset=bass.IndirectOffsetOnAxis(ap=pos[:, par, t:t + 1], axis=0),
                        in_=row[:, par, t, :], in_offset=None).then_inc(rows_out[par], 16)

            pipeline(pool, dict(a_qkv=a_qkv, a_split=a_split, b_unit=b_unit, c_y=c_y, d_ln=d_ln, d_split=d_split,
                                f_pv=f_pv, f_y=f_y, f_scatter=f_scatter))

            wait(pool, r_v, At(1, 0, 0), "pad", apart=v_setup)
            for e in range(E):
                pool.indirect_dma_start(
                    out=routed, out_offset=bass.IndirectOffsetOnAxis(ap=padpos[:, e:e + 1], axis=0),
                    in_=padrow[:, :], in_offset=None).then_inc(pads_out, 16)

            def down(s, q):
                wait(pool, z_v, s, "ve", apart=v_setup)
                nc.gpsimd.tensor_tensor(t_rs[:, q % 2, :], t_ve[:, q % 2, :], half[:, 0:1], ALU.pow
                                        ).then_inc(rstd_p.sem, 1)

            def y(s, q):
                wait(pool, y_v, s, "y", apart=v_setup)
                pool.indirect_dma_start(
                    out=out_d, out_offset=bass.IndirectOffsetOnAxis(ap=t_idx[:, q:q + 1], axis=0),
                    in_=t_y[:, q, :], in_offset=None, bounds_check=TOK - 1, oob_is_err=False
                ).then_inc(y_out[q], 16)

            experts(pool, dict(down=down, y=y))


_INS = ["L0_attn_x", "L0_attn_w_q", "L0_attn_w_k", "L0_attn_w_v", "L0_attn_w_o", "L0_ffn_ln1_g", "L0_ffn_ln1_b",
        "L0_ffn_ln2_g", "L0_ffn_ln2_b", "L0_ffn_wq", "L0_ffn_bq", "L0_ffn_wk", "L0_ffn_bk", "L0_ffn_wv",
        "L0_ffn_bv", "L0_ffn_wo", "L0_ffn_bo", "L0_ffn_gate_w", "L0_ffn_gate_b", "L0_ffn_w1", "L0_ffn_b1",
        "L0_ffn_w2", "L0_ffn_b2"]


def kernel(**inputs):
    import concourse.bacc as bacc
    from concourse.bass_utils import run_bass_kernel_spmd

    nc = bacc.Bacc("TRN2", target_bir_lowering=False, num_devices=1)
    arrays, args = {}, []
    for name, a in [(k, inputs[k]) for k in _INS] + list(constants().items()):
        a = np.ascontiguousarray(a)
        arrays[f"in_{name}"] = a
        args.append(nc.dram_tensor(f"in_{name}", a.shape, mybir.dt.from_np(a.dtype), kind="ExternalInput").ap())
    out = nc.dram_tensor("out_0", (B, S, D), F32, kind="ExternalOutput").ap()
    post_ln_block(nc, *args, out)
    r = run_bass_kernel_spmd(nc, [arrays], core_ids=[0])
    return r.results[0]["out_0"]
```
